# Optimizing a Trainium2 kernel written in Bass

```python
import numpy as np
import jax
import jax.numpy as jnp

def _softmax(x, axis=-1):
    return jax.nn.softmax(x, axis=axis)

def _gelu(x):
    return jax.nn.gelu(x, approximate=True)

def _silu(x):
    return jax.nn.silu(x)

def _sigmoid(x):
    return jax.nn.sigmoid(x)

def _layernorm(x, axis=-1, eps=1e-05):
    m = jnp.mean(x, axis=axis, keepdims=True)
    v = jnp.var(x, axis=axis, keepdims=True)
    return (x - m) / jnp.sqrt(v + eps)

def _scatter_add(tgt, idx, src, axis=0):
    return tgt.at[idx].add(src)

def _segment_sum(src, seg, n):
    return jax.ops.segment_sum(src, seg, n)
kernel_name = 'mk_recurrent_d2_jaxref_r8_545880'

def setup_inputs(seed: int=0):
    np.random.seed(seed)
    _w = jnp.asarray

    def _L0_attn_setup():
        import jax, jax.numpy as jnp
        import numpy as np
        B, N, D_IN, D_OUT = (4, 256, 128, 128)
        key = jax.random.key(seed)
        k = jax.random.split(key, 6)
        x = jax.random.normal(k[0], (B, N, D_IN), dtype=jnp.float32)
        sc_in = 1.0 / np.sqrt(D_IN)
        sc_out = 1.0 / np.sqrt(D_OUT)
        W_spin = jax.random.uniform(k[1], (D_OUT, D_IN), jnp.float32, -sc_in, sc_in)
        b_spin = jax.random.uniform(k[2], (D_OUT,), jnp.float32, -sc_in, sc_in)
        W_global = jax.random.uniform(k[3], (D_OUT, D_OUT), jnp.float32, -sc_out, sc_out)
        W_J = jax.random.uniform(k[4], (D_OUT, D_OUT), jnp.float32, -sc_out, sc_out)
        beta = jnp.ones((1,), dtype=jnp.float32)
        return {'x': x, 'W_spin': W_spin, 'b_spin': b_spin, 'W_global': W_global, 'W_J': W_J, 'beta': beta}
    _L0_attn_in = _L0_attn_setup()

    def _L0_ffn_setup():
        import jax, jax.numpy as jnp
        import numpy as np
        DIM = 128

        def _reference_tuple_inner(x, W_r, W_k, W_v, mu_r, mu_k):
            B, T, C = x.shape
            x_prev = jnp.concatenate([jnp.zeros((B, 1, C), x.dtype), x[:, :-1, :]], axis=1)
            xr = mu_r * x + (1.0 - mu_r) * x_prev
            xk = mu_k * x + (1.0 - mu_k) * x_prev
            r = jax.nn.sigmoid(jnp.einsum('btc,dc->btd', xr, W_r))
            k = jnp.einsum('btc,dc->btd', xk, W_k)
            k_act = jnp.square(jax.nn.relu(k))
            out = r * jnp.einsum('btc,dc->btd', k_act, W_v)
            new_state = x[:, -1, :]
            return (out, new_state)
        key = jax.random.key(seed)
        ks = jax.random.split(key, 6)
        B, T, C = (8, 256, DIM)
        x = jax.random.normal(ks[0], (B, T, C), dtype=jnp.float32)
        s = 1.0 / np.sqrt(C)
        W_r = jax.random.uniform(ks[1], (C, C), jnp.float32, -s, s)
        W_k = jax.random.uniform(ks[2], (C, C), jnp.float32, -s, s)
        W_v = jax.random.uniform(ks[3], (C, C), jnp.float32, -s, s)
        mu_r = jax.random.uniform(ks[4], (C,), jnp.float32)
        mu_k = jax.random.uniform(ks[5], (C,), jnp.float32)
        return {'x': x, 'W_r': W_r, 'W_k': W_k, 'W_v': W_v, 'mu_r': mu_r, 'mu_k': mu_k}
    _L0_ffn_in = _L0_ffn_setup()

    def _L1_attn_setup():
        import jax, jax.numpy as jnp
        import numpy as np
        B, T, C, H, VBD = (2, 256, 128, 16, 256)
        KD = C // H
        VD = VBD // H
        EPS = float(np.finfo(np.float32).eps)

        def _inner_mask(seq_len):
            gamma = jnp.log(1.0 - 2.0 ** (-5.0 - jnp.arange(H, dtype=jnp.float32)))
            idx = jnp.arange(seq_len, dtype=jnp.float32)
            diff = idx[:, None] - idx[None, :]
            causal = diff >= 0
            decay = jnp.where(causal, jnp.exp(gamma[:, None, None] * diff), 0.0)
            scale = jnp.sqrt(decay.sum(-1, keepdims=True))
            return decay / scale
        key = jax.random.key(seed)
        ks = jax.random.split(key, 9)
        s = 0.02
        return {'x': jax.random.normal(ks[0], (B, T, C), dtype=jnp.float32), 'W_qk': jax.random.normal(ks[1], (C, 2 * C), dtype=jnp.float32) * s, 'b_qk': jnp.zeros((2 * C,), dtype=jnp.float32), 'W_v': jax.random.normal(ks[2], (C, VBD), dtype=jnp.float32) * s, 'b_v': jnp.zeros((VBD,), dtype=jnp.float32), 'W_g': jax.random.normal(ks[3], (C, VBD), dtype=jnp.float32) * s, 'b_g': jnp.zeros((VBD,), dtype=jnp.float32), 'W_o': jax.random.normal(ks[4], (VBD, C), dtype=jnp.float32) * s, 'b_o': jnp.zeros((C,), dtype=jnp.float32)}
    _L1_attn_in = _L1_attn_setup()

    def _L1_ffn_setup():
        import jax, jax.numpy as jnp
        import numpy as np
        B, SEQ, DIM = (2, 512, 128)
        E, S = (8, 64)
        HID = 4 * DIM
        SCALE = DIM ** 0.5

        def rmsnorm(x, gamma):
            n = jnp.linalg.norm(x, axis=-1, keepdims=True)
            return x / jnp.maximum(n, 1e-12) * SCALE * gamma
        key = jax.random.key(seed)
        ks = jax.random.split(key, 4)
        w_init = lambda k, shape: jax.random.normal(k, shape, dtype=jnp.float32) * 0.02
        return {'x': jax.random.normal(ks[0], (B, SEQ, DIM), dtype=jnp.float32), 'norm_gamma': jnp.ones((DIM,), jnp.float32), 'slot_norm_gamma': jnp.ones((DIM,), jnp.float32), 'slot_embeds': jax.random.normal(ks[1], (E, S, DIM), dtype=jnp.float32), 'w1': w_init(ks[2], (E, DIM, HID)), 'b1': jnp.zeros((E, HID), jnp.float32), 'w2': w_init(ks[3], (E, HID, DIM)), 'b2': jnp.zeros((E, DIM), jnp.float32)}
    _L1_ffn_in = _L1_ffn_setup()
    _d = {'L0_attn_x': _L0_attn_in['x'], 'L0_attn_W_spin': _L0_attn_in['W_spin'], 'L0_attn_b_spin': _L0_attn_in['b_spin'], 'L0_attn_W_global': _L0_attn_in['W_global'], 'L0_attn_W_J': _L0_attn_in['W_J'], 'L0_attn_beta': _L0_attn_in['beta'], 'L0_ffn_W_r': _L0_ffn_in['W_r'], 'L0_ffn_W_k': _L0_ffn_in['W_k'], 'L0_ffn_W_v': _L0_ffn_in['W_v'], 'L0_ffn_mu_r': _L0_ffn_in['mu_r'], 'L0_ffn_mu_k': _L0_ffn_in['mu_k'], 'L1_attn_W_qk': _L1_attn_in['W_qk'], 'L1_attn_b_qk': _L1_attn_in['b_qk'], 'L1_attn_W_v': _L1_attn_in['W_v'], 'L1_attn_b_v': _L1_attn_in['b_v'], 'L1_attn_W_g': _L1_attn_in['W_g'], 'L1_attn_b_g': _L1_attn_in['b_g'], 'L1_attn_W_o': _L1_attn_in['W_o'], 'L1_attn_b_o': _L1_attn_in['b_o'], 'L1_ffn_norm_gamma': _L1_ffn_in['norm_gamma'], 'L1_ffn_slot_norm_gamma': _L1_ffn_in['slot_norm_gamma'], 'L1_ffn_slot_embeds': _L1_ffn_in['slot_embeds'], 'L1_ffn_w1': _L1_ffn_in['w1'], 'L1_ffn_b1': _L1_ffn_in['b1'], 'L1_ffn_w2': _L1_ffn_in['w2'], 'L1_ffn_b2': _L1_ffn_in['b2']}
    _x0 = _d['L0_attn_x']
    _d['L0_attn_x'] = jax.random.normal(jax.random.fold_in(jax.random.key(seed), 1), (32, 256, 128), dtype=_x0.dtype)
    del _x0
    return _d

def reference(L0_attn_x, L0_attn_W_spin, L0_attn_b_spin, L0_attn_W_global, L0_attn_W_J, L0_attn_beta, L0_ffn_W_r, L0_ffn_W_k, L0_ffn_W_v, L0_ffn_mu_r, L0_ffn_mu_k, L1_attn_W_qk, L1_attn_b_qk, L1_attn_W_v, L1_attn_b_v, L1_attn_W_g, L1_attn_b_g, L1_attn_W_o, L1_attn_b_o, L1_ffn_norm_gamma, L1_ffn_slot_norm_gamma, L1_ffn_slot_embeds, L1_ffn_w1, L1_ffn_b1, L1_ffn_w2, L1_ffn_b2):

    def _L0_attn_ref(x, W_spin, b_spin, W_global, W_J, beta):
        import jax, jax.numpy as jnp
        import numpy as np
        B, N, D_IN, D_OUT = (4, 256, 128, 128)
        s = jnp.einsum('bni,oi->bno', x, W_spin) + b_spin
        mean_field = jnp.mean(s, axis=1, keepdims=True)
        global_influence = jnp.einsum('bmd,od->bmo', mean_field, W_global)
        energy_fields = jnp.einsum('bnd,od->bno', s, W_J)
        scale = 1.0 / jnp.sqrt(jnp.float32(s.shape[2]))
        scores = jnp.einsum('bnd,bmd->bnm', energy_fields, s) * scale
        affinities = jax.nn.softmax(scores, axis=-1)
        local_field = jnp.einsum('bnm,bmd->bnd', affinities, s)
        return jnp.tanh(beta * (s + global_influence + local_field))

    def _L0_ffn_ref(x, W_r, W_k, W_v, mu_r, mu_k):
        import jax, jax.numpy as jnp
        import numpy as np
        DIM = 128

        def _reference_tuple_inner(x, W_r, W_k, W_v, mu_r, mu_k):
            B, T, C = x.shape
            x_prev = jnp.concatenate([jnp.zeros((B, 1, C), x.dtype), x[:, :-1, :]], axis=1)
            xr = mu_r * x + (1.0 - mu_r) * x_prev
            xk = mu_k * x + (1.0 - mu_k) * x_prev
            r = jax.nn.sigmoid(jnp.einsum('btc,dc->btd', xr, W_r))
            k = jnp.einsum('btc,dc->btd', xk, W_k)
            k_act = jnp.square(jax.nn.relu(k))
            out = r * jnp.einsum('btc,dc->btd', k_act, W_v)
            new_state = x[:, -1, :]
            return (out, new_state)
        return _reference_tuple_inner(x, W_r, W_k, W_v, mu_r, mu_k)[0]

    def _L1_attn_ref(x, W_qk, b_qk, W_v, b_v, W_g, b_g, W_o, b_o):
        import jax, jax.numpy as jnp
        import numpy as np
        B, T, C, H, VBD = (2, 256, 128, 16, 256)
        KD = C // H
        VD = VBD // H
        EPS = float(np.finfo(np.float32).eps)

        def _inner_mask(seq_len):
            gamma = jnp.log(1.0 - 2.0 ** (-5.0 - jnp.arange(H, dtype=jnp.float32)))
            idx = jnp.arange(seq_len, dtype=jnp.float32)
            diff = idx[:, None] - idx[None, :]
            causal = diff >= 0
            decay = jnp.where(causal, jnp.exp(gamma[:, None, None] * diff), 0.0)
            scale = jnp.sqrt(decay.sum(-1, keepdims=True))
            return decay / scale
        Bx, Tx, _ = x.shape
        qk = x @ W_qk + b_qk
        q, k = jnp.split(qk, 2, axis=-1)
        v = x @ W_v + b_v
        q = q.reshape(Bx, Tx, H, KD).transpose(0, 2, 1, 3)
        k = k.reshape(Bx, Tx, H, KD).transpose(0, 2, 1, 3)
        v = v.reshape(Bx, Tx, H, VD).transpose(0, 2, 1, 3)
        mask = _inner_mask(Tx)
        scores = jnp.einsum('bhtd,bhsd->bhts', q, k) * mask
        denom = jnp.clip(jnp.abs(scores).sum(-1, keepdims=True), 1.0, 50000.0)
        scores = scores / denom
        ret = jnp.einsum('bhts,bhsv->bthv', scores, v)
        ret = ret * jax.lax.rsqrt(jnp.mean(ret * ret, axis=-1, keepdims=True) + EPS)
        y = ret.reshape(Bx, Tx, H * VD)
        gated = (x @ W_g + b_g) * y
        return gated @ W_o + b_o

    def _L1_ffn_ref(x, norm_gamma, slot_norm_gamma, slot_embeds, w1, b1, w2, b2):
        import jax, jax.numpy as jnp
        import numpy as np
        B, SEQ, DIM = (2, 512, 128)
        E, S = (8, 64)
        HID = 4 * DIM
        SCALE = DIM ** 0.5

        def rmsnorm(x, gamma):
            n = jnp.linalg.norm(x, axis=-1, keepdims=True)
            return x / jnp.maximum(n, 1e-12) * SCALE * gamma
        xn = rmsnorm(x, norm_gamma)
        sn = rmsnorm(slot_embeds, slot_norm_gamma)
        logits = jnp.einsum('bnd,esd->bnes', xn, sn)
        dispatch = jax.nn.softmax(logits, axis=1)
        b, n, e, s = logits.shape
        combine = jax.nn.softmax(logits.reshape(b, n, e * s), axis=-1)
        slots = jnp.einsum('bnd,bnes->besd', xn, dispatch)
        h = jnp.einsum('besd,edh->besh', slots, w1) + b1[None, :, None, :]
        h = jax.nn.gelu(h, approximate=False)
        eo = jnp.einsum('besh,ehd->besd', h, w2) + b2[None, :, None, :]
        eo = eo.reshape(b, e * s, DIM)
        out = jnp.einsum('bmd,bnm->bnd', eo, combine)
        return out
    x = L0_attn_x
    xn = _layernorm(x, axis=-1)
    s = _L0_attn_ref(xn, L0_attn_W_spin, L0_attn_b_spin, L0_attn_W_global, L0_attn_W_J, L0_attn_beta)
    g = _silu(_L0_ffn_ref(xn, L0_ffn_W_r, L0_ffn_W_k, L0_ffn_W_v, L0_ffn_mu_r, L0_ffn_mu_k))
    x = x + s * g
    xn = _layernorm(x, axis=-1)
    s = _L1_attn_ref(xn, L1_attn_W_qk, L1_attn_b_qk, L1_attn_W_v, L1_attn_b_v, L1_attn_W_g, L1_attn_b_g, L1_attn_W_o, L1_attn_b_o)
    g = _silu(_L1_ffn_ref(xn, L1_ffn_norm_gamma, L1_ffn_slot_norm_gamma, L1_ffn_slot_embeds, L1_ffn_w1, L1_ffn_b1, L1_ffn_w2, L1_ffn_b2))
    x = x + s * g
    return x

_drawn_inputs = setup_inputs


def setup_inputs(seed=0):
    import zlib

    import numpy as np

    out = dict(_drawn_inputs(seed))
    spreads = {'L1_attn_b_qk': (0.0, 0.8),
     'L1_attn_b_v': (0.0, 0.8),
     'L1_attn_b_g': (0.0, 0.8),
     'L1_attn_b_o': (0.0, 0.8),
     'L1_ffn_norm_gamma': (1.0, 0.6),
     'L1_ffn_slot_norm_gamma': (1.0, 0.6),
     'L1_ffn_b1': (0.0, 0.8),
     'L1_ffn_b2': (0.0, 0.8)}
    factors = {'L0_attn_W_spin': 2.987,
     'L0_attn_b_spin': 8.0,
     'L0_attn_W_global': 8.0,
     'L0_attn_W_J': 8.0,
     'L0_ffn_W_r': 8.0,
     'L0_ffn_W_k': 3.145,
     'L0_ffn_W_v': 2.909,
     'L0_ffn_mu_r': 8.0,
     'L0_ffn_mu_k': 4.903,
     'L1_attn_W_qk': 8.0,
     'L1_attn_W_v': 8.0,
     'L1_attn_W_g': 8.0,
     'L1_attn_W_o': 8.0,
     'L1_ffn_slot_embeds': 8.0,
     'L1_ffn_w1': 8.0,
     'L1_ffn_w2': 8.0}
    for name, (base, spread) in spreads.items():
        noise = np.random.default_rng([zlib.crc32(name.encode()), seed]).standard_normal(out[name].shape)
        drawn = base * np.exp(spread * noise) if base else spread * noise
        out[name] = jnp.asarray(drawn.astype(out[name].dtype))
    for name, factor in factors.items():
        out[name] = (out[name] * factor).astype(out[name].dtype)
    return out
```

```python
from contextlib import ExitStack

import numpy as np

import concourse.bass as bass
from concourse import mybir

F32 = mybir.dt.float32
ALU = mybir.AluOpType
ACT = mybir.ActivationFunctionType
X = mybir.AxisListType.X

P = 128
C = 128
SEQ = 256
TOK = 2 * SEQ
TILES = TOK // P
HEADS, KD, VD = 16, 8, 16
UNITS = 2 * HEADS
HT = 32
E, SL, HID = 8, 64, 512
ES = E * SL
HC = HID // P
LN_EPS = 1e-5
RET_EPS = float(np.finfo(np.float32).eps)

W_COLS = {}
_at = 0
for _name, _n in (("spin", C), ("J", C), ("global", C), ("r", C), ("k", C), ("v", C),
                  ("q1", C), ("k1", C), ("vg", 2 * HEADS * VD), ("o", 2 * C)):
    W_COLS[_name] = (_at, _at + _n)
    _at += _n
W_N = _at
V_COLS = {}
_at = 0
for _name, _n in (("b_spin", 1), ("mu_r", 1), ("mu_k", 1), ("b_q", 1), ("b_k", 1), ("norm_gamma", 1),
                  ("slot_gamma", 1), ("beta", 1), ("b1", E * HC), ("b2", E), ("b_vg", 2 * HEADS * VD), ("b_o", C)):
    V_COLS[_name] = (_at, _at + _n)
    _at += _n
V_N = _at
K_COLS = {}
_at = 0
for _name, _n in (("ident", P), ("qdecay", SEQ), ("kdecay", SEQ), ("causal", 3 * P), ("head", HEADS), ("count", HT)):
    K_COLS[_name] = (_at, _at + _n)
    _at += _n
K_N = _at

A_USES = [("xnT", "xnT"), ("s", "sT"), ("global", "gbias"), ("e", "eT"), ("srow", "srow"),
          ("score0", "P0"), ("score1", "P1"), ("PT0", "PT0"), ("PT1", "PT1"), ("local", "field"),
          ("r", "rt"), ("k", "kr"), ("v", "rv"), ("prod", "x1"), ("xn2T", "xn2T"), ("xn3T", "xn3T")]

FIRST = [("qk", 0), ("qk", 1), ("L", 0), ("L", 1), ("LT", 0), ("vg", 0)]
SLOTS = [
    [("CT", 0)],
    [("CT", 1), ("LT", 1)],
    [("vg", 1), ("L", 2), ("a_norm", 0)],
    [("L", 3)],
    [("LT", 2), ("CT", 2)],
    [("LT", 3), ("CT", 3), ("a_xnT", 0)],
    [("DT", 0), ("DT", 1), ("a_s", 0)],
    [("DT", 2), ("vg", 2), ("a_global", 0), ("a_e", 0)],
    [("DT", 3), ("a_srow", 0)],
    [("slots", 0), ("a_score", 0)],
    [("slots", 1), ("a_score", 1)],
    [("vg", 3)],
    [("h", 0), ("a_PT", 0)],
    [("h", 1), ("a_PT", 1)],
    [("eo", 0)],
    [("h", 2), ("a_local", 0)],
    [("eo", 1), ("a_r", 0)],
    [("h", 3), ("a_k", 0)],
    [("eo", 2)],
    [("row", 0), ("h", 4), ("a_v", 0)],
    [("row", 1), ("eo", 3)],
    [("h", 5), ("a_gate", 0)],
    [("eo", 4), ("gate", 0)],
    [("h", 6), ("a_prod", 0)],
    [("gatedT", 0), ("eo", 5)],
    [("h", 7), ("a_xn2", 0)],
    [("o", 0), ("eo", 6)],
    [("a_xn3", 0)],
    [("eo", 7)],
    [("a_xn2T", 0)],
    [("eorow", 0)],
    [("a_xn3T", 0), ("eorow", 1)],
    [],
    [("out", 0)],
    [("out", 1)],
    [],
]
LATE = {0: [("row", 2)], 1: [("row", 3)], 4: [("gate", 1)], 5: [("gatedT", 1), ("o", 1)]}
A_TASKS = [("a_norm", 0), ("a_xnT", 0), ("a_s", 0), ("a_global", 0), ("a_e", 0), ("a_srow", 0),
           ("a_score", 0), ("a_score", 1), ("a_PT", 0), ("a_PT", 1), ("a_local", 0), ("a_r", 0), ("a_k", 0),
           ("a_v", 0), ("a_gate", 0), ("a_prod", 0), ("a_xn2", 0), ("a_xn3", 0), ("a_xn2T", 0), ("a_xn3T", 0)]
READ_BY = {"qk": "qkT", "vg": "vg", "L": "Cexp", "LT": "DTexp", "CT": "CT", "DT": "D", "slots": "slotsT",
           "h": "hpre", "eo": "eoT", "eorow": "eorow", "out": "z"}
C_USES = [(f"{n}{k}", (READ_BY[n], k)) for n, k in FIRST + [t for slot in SLOTS for t in slot] if n in READ_BY]
R_USES = [("g0", ("RT", 0)), ("g1", ("RT", 1)), ("g2", ("RT", 2)), ("g3", ("RT", 3)), ("row0", ("U", 0)),
          ("row1", ("U", 1)), ("g4", ("RT", 4)), ("gatedT0", ("gatedT", 0)), ("g5", ("RT", 5)), ("o0", ("attn", 0)),
          ("g6", ("RT", 6)), ("g7", ("RT", 7)), ("row2", ("U", 2)), ("row3", ("U", 3)), ("gatedT1", ("gatedT", 1)),
          ("o1", ("attn", 1))]


class Signal:

    def __init__(self, sem, per=1, by=1):
        self.sem, self.per, self.by = sem, per, by

    def __call__(self, p, k=0):
        return self.sem, (p * self.per + k + 1) * self.by


def build(nc, x, weights, vectors, consts, w1, w2, slot_rows, out):
    pairs = x.shape[0] // TOK
    with ExitStack() as ctx:
        def sb(name, *shape):
            return ctx.enter_context(nc.sbuf_tensor(name, [P, *shape], F32))

        def signal(name, per=1, by=1):
            return Signal(ctx.enter_context(nc.semaphore(name)), per, by)

        w_sb, v_sb, k_sb = sb("w_sb", W_N), sb("v_sb", V_N), sb("k_sb", K_N)
        w1_sb, w2_sb = sb("w1_sb", E, HID), sb("w2_sb", E, HC, C)
        slot_sb, slot_sq, snT = sb("slot_sb", 4, C), sb("slot_sq", C), sb("snT", ES)
        slot_n = sb("slot_n", 3, 4)
        mu1 = sb("mu1", 2)
        gamma2 = sb("gamma2", 1)
        mhalf, ln_eps = sb("mhalf", HEADS), sb("ln_eps", TILES)
        W = {n: w_sb[:, a:b] for n, (a, b) in W_COLS.items()}
        V = {n: v_sb[:, a:b] for n, (a, b) in V_COLS.items()}
        K = {n: k_sb[:, a:b] for n, (a, b) in K_COLS.items()}
        ident, causal = K["ident"], K["causal"]

        x_sb = sb("x_sb", TILES, C)
        stat, mv = sb("stat", TILES, 6), sb("mv", TILES, 2)
        var_eps, rstd = sb("var_eps", TILES), sb("rstd", TILES)
        xn = sb("xn", TILES, C)
        xnT = sb("xnT", 2, SEQ + 1)
        mix = sb("mix", 2, 2, SEQ)
        xrT, xkT = mix[:, 0], mix[:, 1]
        sT, s_sum, gbias = sb("sT", 2, SEQ), sb("s_sum", 2), sb("gbias", 2)
        eT, srow = sb("eT", TOK), sb("srow", TILES, C)
        smax, snmax, ssum, srec = sb("smax", TILES), sb("snmax", TILES), sb("ssum", TILES), sb("srec", TILES)
        prob, probT = sb("prob", TILES, SEQ), sb("probT", 2, TOK)
        spinT = sb("spinT", 2, SEQ)
        field = sT
        rt, kr = eT[:], srow[:].rearrange("p j c -> p (j c)")
        rv, rvt = prob[:, 0:2].rearrange("p j m -> p (j m)"), prob[:, 2:4].rearrange("p j m -> p (j m)")
        prodT = spinT[:].rearrange("p b n -> p (b n)")
        stat2, mv2 = sb("stat2", TILES, 6), sb("mv2", TILES, 2)
        var_eps2, rstd2 = sb("var_eps2", TILES), sb("rstd2", TILES)
        xn2, sq2 = sb("xn2", TILES, C), sb("sq2", C)
        norm2, norm2c, rnorm = sb("norm2", TILES), sb("norm2c", TILES), sb("rnorm", TILES)
        x1 = [sb(f"x1_{i}", TILES, C) for i in range(2)]
        xn2T, xn3, xn3T = sb("xn2T", 2, SEQ), sb("xn3", TILES, C), sb("xn3T", TOK)

        qT, kT = sb("qT", 2, SEQ), sb("kT", 2, SEQ)
        KM, LEAD, MR = 6, 4, 8
        km = sb("km", KM, SEQ)
        vrow, grow = sb("vrow", TILES, HEADS, HT), sb("grow", TILES, HEADS, VD)
        ret, ret_abs = sb("ret", MR, 3 * P), sb("ret_abs", MR, 3 * P)
        RT = sb("RT", 4, SEQ)
        U = sb("U", 2, HEADS, HT)
        usq, ug = sb("usq", 2, HEADS, VD), sb("ug", 2, HEADS, VD)
        ums, den, den2, uvar, urs = (sb(n, 2, HEADS) for n in ("ums", "den", "den2", "uvar", "urs"))
        gated = sb("gated", 2, HEADS * VD)
        gatedT = sb("gatedT", 2, 2, P)
        gatedT2 = sb("gatedT2", 2, 2, P)
        attn = sb("attn", TILES, C)

        lmax, csum, crec = sb("lmax", TILES), sb("csum", TILES), sb("crec", TILES)
        crow, cT = sb("crow", 2, ES), sb("cT", 4, TOK)
        ltmax, dsum, drec = sb("ltmax", 4, 2), sb("dsum", 4, 2), sb("drec", 4, 2)
        dT, d = sb("dT", 4, 2, SEQ), sb("d", TILES, ES)
        slotsT = sb("slotsT", E, 2, SL)
        hact = sb("hact", 2, HC, P)
        eoT, eorow = sb("eoT", 2, E, SL), sb("eorow", 2, 4, C)
        z, zt, x2 = (sb(n, TILES, C) for n in ("z", "zt", "x2"))

        banks = [ctx.enter_context(nc.psum_tensor(f"bank{i}", [P, 512], F32)) for i in range(8)]
        bank_a, bank_c, bank_s, bank_r = banks[0:2], banks[2:4], banks[4:6], banks[6:8]
        filled_a = [signal(f"filled_a{i}", len(A_USES) // 2) for i in range(2)]
        filled_c = [signal(f"filled_c{i}", len(C_USES) // 2) for i in range(2)]
        filled_s = [signal(f"filled_s{i}", UNITS // 2) for i in range(2)]
        filled_r = [signal(f"filled_r{i}", len(R_USES) // 2) for i in range(2)]
        assert len(A_USES) % 2 == 0 and len(C_USES) % 2 == 0
        a_index = {n: i for i, (n, _) in enumerate(A_USES)}
        c_index = {n: i for i, (n, _) in enumerate(C_USES)}
        r_index = {n: i for i, (n, _) in enumerate(R_USES)}

        loaded = signal("loaded", by=16)
        loaded2 = signal("loaded2", by=16)
        x_in = signal("x_in", by=16)
        ready = {}
        for name, per in (
            ("setup", 3), ("derived", 3), ("slot_ready", 4), ("slot_sqs", 1), ("slot_rn", 3), ("slot_norm", 1),
            ("stat", 1), ("mv", 1), ("var_eps", 1), ("rstd", 1), ("xn", 1), ("xnT", 1), ("mix_a", 1), ("mix", 1),
            ("sT", 1), ("gbias", 1), ("eT", 1), ("srow", 1), ("smax", 2), ("snmax", 2), ("P", 2), ("srec", 2),
            ("Pn", 2), ("PT", 2), ("field", 1), ("spinT", 1), ("rt", 1), ("kr", 1), ("ka", 1), ("rv", 1),
            ("snT", 1), ("rvt", 1), ("rvg", 1), ("prodT", 1), ("x1", 1), ("stat2", 1), ("mv2", 1), ("var_eps2", 1),
            ("rstd2", 1), ("xn2", 1), ("norm2", 1), ("norm2c", 1), ("rnorm", 1), ("xn3", 1), ("xn2T", 1),
            ("xn3T", 1), ("qkT", 2), ("km", UNITS), ("vg", TILES), ("ret", UNITS), ("ret_abs", UNITS),
            ("RT", UNITS // 4), ("U", TILES), ("usq", TILES), ("ums", TILES), ("den", TILES), ("den2", TILES),
            ("uvar", TILES), ("urs", TILES), ("ug", TILES), ("gated", TILES), ("gatedT", 2), ("attn", 2),
            ("lmax", TILES), ("Cexp", TILES), ("CT", TILES), ("ltmax", 4), ("DTexp", 4), ("drec", 4),
            ("DTn", 4), ("D", 4), ("slotsT", 2), ("hpre", E), ("hact", E), ("eoT", E), ("eorow", 2),
            ("crec", 1), ("z", 2), ("zt", 2), ("zg", 2), ("sg", 1), ("x2", 1),
        ):
            ready[name] = signal(f"{name}_ready", per)
        stored = signal("stored", by=16)
        filled_setup = signal("filled_setup")
        passed = {"vector": signal("passed_vector"), "gpsimd": signal("passed_gpsimd")}
        sq2_ready = signal("sq2_ready", TILES - 1)

        def a_bank(name):
            i = a_index[name]
            return bank_a[i % 2], filled_a[i % 2], i // 2

        def c_bank(name):
            i = c_index[name]
            return bank_c[i % 2], filled_c[i % 2], i // 2

        def r_bank(name):
            i = r_index[name]
            return bank_r[i % 2], filled_r[i % 2], i // 2

        def r_read(name):
            i = r_index[name] - 2
            base, k = R_USES[i % len(R_USES)][1]
            return ready[base], k, i < 0

        def a_read(name):
            i = a_index[name] - 2
            back = i < 0
            done = A_USES[i % len(A_USES)][1]
            base, k = (done[:-1], int(done[-1])) if done[:-1] in ("P", "PT") and done[-1] in "01" else (done, 0)
            return ready[base], k, back

        def c_read(name):
            i = c_index[name] - 2
            base, k = C_USES[i % len(C_USES)][1]
            return ready[base], k, i < 0

        def first(p):
            return isinstance(p, int) and p == 0

        def schedule(prologue, step, end, eng):
            prologue()
            step(0, 0, True)
            with eng.Fori(0, pairs // 2 - 1) as i:
                step(2 * i + 1, 1, True)
                step(2 * i + 2, 0, True)
            step(pairs - 1, 1, False)
            end(pairs - 1, 1)

        def steps_of(eng, tasks, head):
            def prologue():
                for name, k in A_TASKS:
                    if name in tasks:
                        tasks[name](0, 0, k)

            def step(p, par, next_a):
                def run(name, k):
                    if name not in tasks:
                        return
                    if not name.startswith("a_"):
                        tasks[name](p, par, k)
                    elif next_a:
                        tasks[name](p + 1, 1 - par, k)

                for name, k in FIRST:
                    run(name, k)
                for u, slot in enumerate(SLOTS):
                    head(p, u)
                    if not first(p):
                        late(p - 1, 1 - par, u)
                    for name, k in slot:
                        run(name, k)

            def late(p, par, u):
                for name, k in LATE.get(u, []):
                    if name in tasks:
                        tasks[name](p, par, k)

            def end(p, par):
                for u in LATE:
                    late(p, par, u)

            schedule(prologue, step, end, eng)

        block = ctx.enter_context(nc.Block())

        @block.sync
        def _(sp):
            def load_x(p):
                sp.dma_start(x_sb[:], x[bass.ds(p * TOK, TOK), :].rearrange("(j p) c -> p j c", p=P)).then_inc(x_in.sem, 16)

            def store(p):
                sp.wait_ge(*ready["x2"](p))
                sp.dma_start(out[bass.ds(p * TOK, TOK), :].rearrange("(j p) c -> p j c", p=P), x2[:]).then_inc(stored.sem, 16)

            load_x(0)
            sp.sem_inc(stored.sem, 16)
            sp.dma_start(k_sb[:], consts).then_inc(loaded.sem, 16)
            sp.dma_start(w_sb[:], weights).then_inc(loaded.sem, 16)
            sp.dma_start(v_sb[:], vectors).then_inc(loaded.sem, 16)
            sp.dma_start(slot_sb[:], slot_rows).then_inc(loaded.sem, 16)
            sp.dma_start(w1_sb[:], w1).then_inc(loaded2.sem, 16)
            sp.dma_start(w2_sb[:], w2).then_inc(loaded2.sem, 16)
            sp.wait_ge(*ready["x1"](0))
            load_x(1)
            with sp.Fori(0, pairs - 2) as p:
                sp.wait_ge(*ready["x1"](p + 1))
                load_x(p + 2)
                store(p)
            store(pairs - 2)
            store(pairs - 1)
            sp.wait_ge(*stored(pairs))

        @block.gpsimd
        def _(pool):
            pool.memset(ln_eps[:], LN_EPS)
            pool.memset(mhalf[:], -0.5).then_inc(ready["setup"].sem, 1)
            pool.memset(vrow[:], 0.0).then_inc(ready["setup"].sem, 1)
            pool.memset(xnT[:, :, 0:1], 0.0).then_inc(ready["setup"].sem, 1)
            pool.wait_ge(*ready["slot_sqs"](0))
            pool.wait_ge(ready["setup"].sem, 3)
            pool.tensor_scalar(slot_n[:, 1], slot_n[:, 0], 1e-24, None, ALU.max).then_inc(ready["slot_rn"].sem, 1)
            pool.wait_ge(ready["slot_rn"].sem, 1)
            pool.tensor_tensor(slot_n[:, 2], slot_n[:, 1], mhalf[:, 0:4], ALU.pow).then_inc(ready["slot_rn"].sem, 1)

            def a_norm(p, par, k):
                pool.wait_ge(*ready["mv"](p))
                pool.tensor_tensor(var_eps[:], mv[:, :, 1], ln_eps[:], ALU.add).then_inc(ready["var_eps"].sem, 1)
                pool.wait_ge(*ready["var_eps"](p))
                pool.tensor_tensor(rstd[:], var_eps[:], mhalf[:, 0:TILES], ALU.pow).then_inc(ready["rstd"].sem, 1)

            def a_prod(p, par, k):
                pool.wait_ge(*ready["mv2"](p))
                pool.tensor_tensor(var_eps2[:], mv2[:, :, 1], ln_eps[:], ALU.add).then_inc(ready["var_eps2"].sem, 1)
                pool.wait_ge(*ready["var_eps2"](p))
                pool.tensor_tensor(rstd2[:], var_eps2[:], mhalf[:, 0:TILES], ALU.pow).then_inc(ready["rstd2"].sem, 1)

            def a_xn2(p, par, k):
                pool.wait_ge(*ready["norm2c"](p))
                pool.tensor_tensor(rnorm[:], norm2c[:], mhalf[:, 0:TILES], ALU.pow).then_inc(ready["rnorm"].sem, 1)

            def mask_keys(p, u):
                if u >= UNITS:
                    return
                b, h = divmod(u, HEADS)
                pool.wait_ge(*ready["qkT"](p, 1))
                if u >= KM:
                    pool.wait_ge(*filled_s[u % 2](p, (u - KM) // 2))
                elif not first(p):
                    pool.wait_ge(*filled_s[u % 2](p - 1, (u - KM + UNITS) // 2))
                pool.sem_inc(passed["gpsimd"].sem, 1)
                pool.tensor_scalar(km[:, u % KM], kT[:, b], K["head"][:, h:h + 1], 1.0, ALU.mult, ALU.mult)\
                    .then_inc(ready["km"].sem, 1)

            def head(p, u):
                for w in range(LEAD + 1) if u == 0 else [u + LEAD]:
                    mask_keys(p, w)

            def row(p, par, j):
                pool.wait_ge(*ready["uvar"](p, j))
                pool.tensor_tensor(urs[:, j % 2], uvar[:, j % 2], mhalf[:], ALU.pow).then_inc(ready["urs"].sem, 1)

            steps_of(pool, {"a_norm": a_norm, "a_prod": a_prod, "a_xn2": a_xn2, "row": row},
                     head)

        @block.scalar
        def _(act):
            act.wait_ge(loaded.sem, 64)
            for j in range(4):
                if j:
                    act.wait_ge(ready["slot_ready"].sem, j)
                act.activation(slot_sq[:], slot_sb[:, j], ACT.Square, accum_out=slot_n[:, 0, j:j + 1])\
                    .then_inc(ready["slot_ready" if j < 3 else "slot_sqs"].sem, 1)

            def a_filled(name, p):
                bank, filled, k = a_bank(name)
                act.wait_ge(*filled(p, k))
                return bank

            def c_filled(name, p):
                bank, filled, k = c_bank(name)
                act.wait_ge(*filled(p, k))
                return bank

            def r_filled(name, p):
                bank, filled, k = r_bank(name)
                act.wait_ge(*filled(p, k))
                return bank

            def a_xnT(p, par, k):
                bank = a_filled("xnT", p)
                act.activation(xnT[:, :, 1:SEQ + 1], bank[:].rearrange("p (b n) -> p b n", b=2), ACT.Copy)\
                    .then_inc(ready["xnT"].sem, 1)

            def a_s(p, par, k):
                bank = a_filled("s", p)
                for b in range(2):
                    ins = act.activation(sT[:, b], bank[:, b * SEQ:(b + 1) * SEQ], ACT.Identity, bias=V["b_spin"],
                                         accum_out=s_sum[:, b:b + 1])
                ins.then_inc(ready["sT"].sem, 1)

            def a_e(p, par, k):
                bank = a_filled("e", p)
                act.activation(eT[:], bank[:], ACT.Copy).then_inc(ready["eT"].sem, 1)

            def a_score(p, par, b):
                bank = a_filled(f"score{b}", p)
                act.wait_ge(*ready["snmax"](p, b))
                for i in range(2):
                    j = 2 * b + i
                    ins = act.activation(prob[:, j], bank[:, i * SEQ:(i + 1) * SEQ], ACT.Exp, bias=snmax[:, j:j + 1],
                                         scale=C ** -0.5, accum_out=ssum[:, j:j + 1])
                ins.then_inc(ready["P"].sem, 1)

            def a_PT(p, par, m):
                bank = a_filled(f"PT{m}", p)
                act.activation(probT[:, m], bank[:], ACT.Copy).then_inc(ready["PT"].sem, 1)

            def a_local(p, par, k):
                act.wait_ge(*ready["field"](p))
                for b in range(2):
                    ins = act.activation(spinT[:, b], field[:, b], ACT.Tanh, bias=gbias[:, b:b + 1], scale=V["beta"])
                ins.then_inc(ready["spinT"].sem, 1)

            def a_r(p, par, k):
                bank = a_filled("r", p)
                act.activation(rt, bank[:], ACT.Tanh, scale=0.5).then_inc(ready["rt"].sem, 1)

            def a_k(p, par, k):
                bank = a_filled("k", p)
                act.activation(kr, bank[:], ACT.Relu).then_inc(ready["kr"].sem, 1)

            def a_v(p, par, k):
                act.wait_ge(*ready["rv"](p))
                act.activation(rvt, rv, ACT.Tanh, scale=0.25).then_inc(ready["rvt"].sem, 1)

            def a_xn2(p, par, k):
                act.wait_ge(*ready["xn2"](p))
                for j in range(TILES):
                    ins = act.activation(sq2[:], xn2[:, j], ACT.Square, accum_out=norm2[:, j:j + 1])
                    if j < TILES - 1:
                        ins.then_inc(sq2_ready.sem, 1)
                        act.wait_ge(*sq2_ready(p, j))
                ins.then_inc(ready["norm2"].sem, 1)

            def a_xn2T(p, par, k):
                bank = a_filled("xn2T", p)
                act.activation(xn2T[:], bank[:].rearrange("p (b n) -> p b n", b=2), ACT.Copy)\
                    .then_inc(ready["xn2T"].sem, 1)

            def a_xn3T(p, par, k):
                bank = a_filled("xn3T", p)
                act.activation(xn3T[:], bank[:], ACT.Copy).then_inc(ready["xn3T"].sem, 1)

            def L(p, par, j):
                bank = c_filled(f"L{j}", p)
                act.wait_ge(*ready["lmax"](p, j))
                if j >= 2:
                    act.wait_ge(*c_bank(f"CT{j - 2}")[1](p, c_bank(f"CT{j - 2}")[2]))
                act.activation(crow[:, j % 2], bank[:], ACT.Exp, bias=lmax[:, j:j + 1], accum_out=csum[:, j:j + 1])\
                    .then_inc(ready["Cexp"].sem, 1)

            def LT(p, par, m):
                bank = c_filled(f"LT{m}", p)
                act.wait_ge(*ready["ltmax"](p, m))
                for b in range(2):
                    ins = act.activation(dT[:, m, b], bank[:, b * SEQ:(b + 1) * SEQ], ACT.Exp,
                                         bias=ltmax[:, m, b:b + 1], accum_out=dsum[:, m, b:b + 1])
                ins.then_inc(ready["DTexp"].sem, 1)

            def CT(p, par, j):
                bank = c_filled(f"CT{j}", p)
                act.activation(cT[:, :, j * P:(j + 1) * P], bank[:].rearrange("p (m n) -> p m n", m=4), ACT.Copy)\
                    .then_inc(ready["CT"].sem, 1)

            def DT(p, par, m):
                bank = c_filled(f"DT{m}", p)
                act.activation(d[:, :, m * P:(m + 1) * P], bank[:].rearrange("p (j s) -> p j s", j=TILES), ACT.Copy)\
                    .then_inc(ready["D"].sem, 1)

            def slots(p, par, b):
                bank = c_filled(f"slots{b}", p)
                act.activation(slotsT[:, :, b], bank[:].rearrange("p (e s) -> p e s", e=E), ACT.Copy,
                               scale=V["norm_gamma"]).then_inc(ready["slotsT"].sem, 1)

            def h(p, par, e):
                act.wait_ge(*ready["hpre"](p, e))
                act.activation(hact[:, e % 2], hact[:, e % 2], ACT.Gelu).then_inc(ready["hact"].sem, 1)

            def row(p, par, j):
                bank = r_filled(f"row{j}", p)
                act.activation(U[:, j % 2], bank[:].rearrange("p (h v) -> p h v", h=HEADS), ACT.Copy)\
                    .then_inc(ready["U"].sem, 1)
                act.wait_ge(*ready["U"](p, j))
                act.activation(usq[:, j % 2], U[:, j % 2, :, 0:VD], ACT.Square).then_inc(ready["usq"].sem, 1)

            def gatedT_(p, par, b):
                bank = r_filled(f"gatedT{b}", p)
                act.activation((gatedT, gatedT2)[b][:], bank[:].rearrange("p (i v n) -> p i v n", i=2, v=2), ACT.Copy)\
                    .then_inc(ready["gatedT"].sem, 1)

            def eorow_(p, par, b):
                bank = c_filled(f"eorow{b}", p)
                act.activation(eorow[:, b], bank[:].rearrange("p (m c) -> p m c", m=4), ACT.Copy)\
                    .then_inc(ready["eorow"].sem, 1)

            def out_(p, par, b):
                act.wait_ge(*ready["z"](p, b))
                act.activation(zt[:, 2 * b:2 * b + 2], z[:, 2 * b:2 * b + 2], ACT.Tanh, scale=0.5)\
                    .then_inc(ready["zt"].sem, 1)

            def head(p, u):
                if u < UNITS:
                    act.wait_ge(*ready["ret"](p, u))
                    if u >= MR:
                        g = u // 4 - MR // 4
                        _, filled, k = r_bank(f"g{g}")
                        act.wait_ge(*filled(p, k))
                    act.activation(ret_abs[:, u % MR], ret[:, u % MR], ACT.Abs).then_inc(ready["ret_abs"].sem, 1)
                g = (u - 7) // 4
                if u >= 7 and (u - 7) % 4 == 0 and g < UNITS // 4:
                    bank = r_filled(f"g{g}", p)
                    act.activation(RT[:, g % 4], bank[:, 0:SEQ], ACT.Copy).then_inc(ready["RT"].sem, 1)

            steps_of(act, {"a_xnT": a_xnT, "a_s": a_s, "a_e": a_e, "a_score": a_score, "a_PT": a_PT,
                           "a_local": a_local, "a_r": a_r, "a_k": a_k, "a_v": a_v, "a_xn2": a_xn2,
                           "a_xn2T": a_xn2T, "a_xn3T": a_xn3T, "L": L, "LT": LT, "CT": CT, "DT": DT,
                           "slots": slots, "h": h, "row": row, "gatedT": gatedT_, "eorow": eorow_, "out": out_}, head)

        @block.vector
        def _(dve):
            dve.wait_ge(loaded.sem, 64)
            dve.tensor_scalar(mu1[:, 0:1], V["mu_r"], -1.0, 1.0, ALU.mult, ALU.add).then_inc(ready["derived"].sem, 1)
            dve.tensor_scalar(mu1[:, 1:2], V["mu_k"], -1.0, 1.0, ALU.mult, ALU.add).then_inc(ready["derived"].sem, 1)
            dve.tensor_tensor(gamma2[:], V["norm_gamma"], V["slot_gamma"], ALU.mult).then_inc(ready["derived"].sem, 1)
            dve.wait_ge(ready["slot_rn"].sem, 2)
            for j in range(4):
                ins = dve.tensor_scalar(slot_sb[:, j], slot_sb[:, j], slot_n[:, 2, j:j + 1], float(C) ** 0.5,
                                        ALU.mult, ALU.mult)
            ins.then_inc(ready["slot_norm"].sem, 1)
            dve.wait_ge(ready["derived"].sem, 3)
            dve.wait_ge(filled_setup.sem, 1)
            dve.tensor_scalar(snT[:], bank_r[1][:], gamma2[:, 0:1], None, ALU.mult)\
               .then_inc(ready["snT"].sem, 1)

            def a_filled(name, p):
                bank, filled, k = a_bank(name)
                dve.wait_ge(*filled(p, k))
                return bank

            def c_filled(name, p):
                bank, filled, k = c_bank(name)
                dve.wait_ge(*filled(p, k))
                return bank

            def moments(src, stat, mv, name, mv_name, p):
                for j in range(TILES):
                    ins = dve.bn_stats(stat[:, j], src[:, j])
                ins.then_inc(ready[name].sem, 1)
                dve.wait_ge(*ready[name](p))
                dve.sem_inc(passed["vector"].sem, 1)
                for j in range(TILES):
                    ins = dve.bn_aggr(mv[:, j], stat[:, j])
                ins.then_inc(ready[mv_name].sem, 1)

            def a_norm(p, par, k):
                dve.wait_ge(*x_in(p))
                moments(x_sb, stat, mv, "stat", "mv", p)
                dve.wait_ge(*ready["rstd"](p))
                for j in range(TILES):
                    ins = dve.tensor_scalar(xn[:, j], x_sb[:, j], mv[:, j, 0:1], rstd[:, j:j + 1],
                                            ALU.subtract, ALU.mult)
                ins.then_inc(ready["xn"].sem, 1)

            def a_xnT(p, par, k):
                dve.wait_ge(*ready["xnT"](p))
                for i in range(2):
                    ins = dve.tensor_scalar(mix[:, i], xnT[:, :, 0:SEQ], mu1[:, i:i + 1], None, ALU.mult)
                ins.then_inc(ready["mix_a"].sem, 1)
                dve.wait_ge(*ready["mix_a"](p))
                for i, mu in enumerate(("mu_r", "mu_k")):
                    ins = dve.scalar_tensor_tensor(out=mix[:, i], in0=xnT[:, :, 1:SEQ + 1], scalar=V[mu],
                                                   in1=mix[:, i], op0=ALU.mult, op1=ALU.add)
                ins.then_inc(ready["mix"].sem, 1)

            def a_global(p, par, k):
                bank = a_filled("global", p)
                dve.tensor_scalar(gbias[:], bank[:, 0:2], V["beta"], 1.0 / SEQ, ALU.mult, ALU.mult)\
                   .then_inc(ready["gbias"].sem, 1)

            def a_srow(p, par, k):
                bank = a_filled("srow", p)
                dve.tensor_copy(srow[:], bank[:].rearrange("p (j c) -> p j c", j=TILES)).then_inc(ready["srow"].sem, 1)

            def norm_prob(p, b):
                dve.wait_ge(*ready["P"](p, b))
                dve.reciprocal(srec[:, 2 * b:2 * b + 2], ssum[:, 2 * b:2 * b + 2]).then_inc(ready["srec"].sem, 1)
                dve.wait_ge(*ready["srec"](p, b))
                for j in (2 * b, 2 * b + 1):
                    ins = dve.tensor_scalar(prob[:, j], prob[:, j], srec[:, j:j + 1], None, ALU.mult)
                ins.then_inc(ready["Pn"].sem, 1)

            def a_score(p, par, b):
                bank = a_filled(f"score{b}", p)
                dve.tensor_reduce(smax[:, 2 * b:2 * b + 2], bank[:].rearrange("p (i m) -> p i m", i=2), X, ALU.max)\
                   .then_inc(ready["smax"].sem, 1)
                dve.wait_ge(*ready["smax"](p, b))
                dve.tensor_scalar(snmax[:, 2 * b:2 * b + 2], smax[:, 2 * b:2 * b + 2], -(C ** -0.5), None, ALU.mult)\
                   .then_inc(ready["snmax"].sem, 1)
                if b:
                    norm_prob(p, 0)

            def a_PT(p, par, m):
                if m == 0:
                    norm_prob(p, 1)

            def a_local(p, par, k):
                bank = a_filled("local", p)
                dve.tensor_tensor(field[:], bank[:].rearrange("p (b n) -> p b n", b=2), sT[:], ALU.add)\
                   .then_inc(ready["field"].sem, 1)

            def a_k(p, par, k):
                dve.wait_ge(*ready["kr"](p))
                dve.tensor_tensor(kr, kr, kr, ALU.mult).then_inc(ready["ka"].sem, 1)

            def a_v(p, par, k):
                bank = a_filled("v", p)
                dve.wait_ge(*ready["rt"](p))
                dve.scalar_tensor_tensor(out=rv, in0=rt, scalar=1.0, in1=bank[:], op0=ALU.add, op1=ALU.mult)\
                   .then_inc(ready["rv"].sem, 1)

            def a_gate(p, par, k):
                dve.wait_ge(*ready["rvt"](p))
                dve.scalar_tensor_tensor(out=rvt, in0=rvt, scalar=1.0, in1=rv, op0=ALU.add, op1=ALU.mult)\
                   .then_inc(ready["rvg"].sem, 1)
                dve.wait_ge(*ready["rvg"](p))
                dve.wait_ge(*ready["spinT"](p))
                dve.scalar_tensor_tensor(out=prodT, in0=prodT, scalar=0.25,
                                         in1=rvt, op0=ALU.mult, op1=ALU.mult).then_inc(ready["prodT"].sem, 1)

            def a_prod(p, par, k):
                bank = a_filled("prod", p)
                dve.tensor_tensor(x1[par][:], bank[:].rearrange("p (j c) -> p j c", j=TILES), x_sb[:], ALU.add)\
                   .then_inc(ready["x1"].sem, 1)
                dve.wait_ge(*ready["x1"](p))
                moments(x1[par], stat2, mv2, "stat2", "mv2", p)

            def a_xn2(p, par, k):
                dve.wait_ge(*ready["rstd2"](p))
                for j in range(TILES):
                    ins = dve.tensor_scalar(xn2[:, j], x1[par][:, j], mv2[:, j, 0:1], rstd2[:, j:j + 1],
                                            ALU.subtract, ALU.mult)
                ins.then_inc(ready["xn2"].sem, 1)
                dve.wait_ge(*ready["norm2"](p))
                dve.tensor_scalar(norm2c[:], norm2[:], 1e-24, None, ALU.max).then_inc(ready["norm2c"].sem, 1)

            def a_xn3(p, par, k):
                dve.wait_ge(*ready["rnorm"](p))
                for j in range(TILES):
                    ins = dve.tensor_scalar(xn3[:, j], xn2[:, j], rnorm[:, j:j + 1], C ** 0.5, ALU.mult, ALU.mult)
                ins.then_inc(ready["xn3"].sem, 1)

            def qk(p, par, k):
                bank = c_filled(f"qk{k}", p)
                dst, bias, decay = ((qT, "b_q", "qdecay"), (kT, "b_k", "kdecay"))[k]
                dve.scalar_tensor_tensor(out=dst[:], in0=bank[:].rearrange("p (b n) -> p b n", b=2), scalar=V[bias],
                                         in1=K[decay].unsqueeze(1).broadcast_to([P, 2, SEQ]),
                                         op0=ALU.add, op1=ALU.mult).then_inc(ready["qkT"].sem, 1)

            def vg(p, par, j):
                bank = c_filled(f"vg{j}", p)
                n = HEADS * VD
                dve.tensor_tensor(vrow[:, j, :, 0:VD], bank[:, 0:n].rearrange("p (h v) -> p h v", h=HEADS),
                                  V["b_vg"][:, 0:n].rearrange("p (h v) -> p h v", h=HEADS), ALU.add)
                dve.tensor_tensor(grow[:, j], bank[:, n:2 * n].rearrange("p (h v) -> p h v", h=HEADS),
                                  V["b_vg"][:, n:2 * n].rearrange("p (h v) -> p h v", h=HEADS), ALU.add)\
                   .then_inc(ready["vg"].sem, 1)

            def L(p, par, j):
                bank = c_filled(f"L{j}", p)
                dve.tensor_reduce(lmax[:, j:j + 1], bank[:], X, ALU.max, negate=True).then_inc(ready["lmax"].sem, 1)

            def norm_dispatch(p, m):
                dve.wait_ge(*ready["DTexp"](p, m))
                dve.reciprocal(drec[:, m], dsum[:, m]).then_inc(ready["drec"].sem, 1)
                dve.wait_ge(*ready["drec"](p, m))
                for b in range(2):
                    ins = dve.tensor_scalar(dT[:, m, b], dT[:, m, b], drec[:, m, b:b + 1], None, ALU.mult)
                ins.then_inc(ready["DTn"].sem, 1)

            def LT(p, par, m):
                bank = c_filled(f"LT{m}", p)
                dve.tensor_reduce(ltmax[:, m], bank[:].rearrange("p (b n) -> p b n", b=2), X, ALU.max, negate=True)\
                   .then_inc(ready["ltmax"].sem, 1)
                if m:
                    norm_dispatch(p, m - 1)

            def DT(p, par, m):
                if m == 0:
                    norm_dispatch(p, 3)

            def h(p, par, e):
                bank = c_filled(f"h{e}", p)
                if e >= 2:
                    _, filled, k = c_bank(f"eo{e - 2}")
                    dve.wait_ge(*filled(p, k))
                dve.tensor_tensor(hact[:, e % 2], bank[:].rearrange("p (c n) -> p c n", c=HC),
                                  V["b1"][:, e * HC:(e + 1) * HC].unsqueeze(2).broadcast_to([P, HC, P]), ALU.add)\
                   .then_inc(ready["hpre"].sem, 1)

            def eo(p, par, e):
                bank = c_filled(f"eo{e}", p)
                dve.tensor_scalar(eoT[:, :, e], bank[:, 0:P].rearrange("p (b s) -> p b s", b=2), V["b2"][:, e:e + 1],
                                  None, ALU.add).then_inc(ready["eoT"].sem, 1)

            def row(p, par, j):
                i = j % 2
                dve.wait_ge(*ready["U"](p, j))
                dve.tensor_scalar(den[:, i], U[:, i, :, VD], 1.0, 50000.0, ALU.max, ALU.min).then_inc(ready["den"].sem, 1)
                dve.tensor_tensor(ug[:, i], U[:, i, :, 0:VD], grow[:, j], ALU.mult).then_inc(ready["ug"].sem, 1)
                dve.wait_ge(*ready["den"](p, j))
                dve.scalar_tensor_tensor(out=den2[:, i], in0=den[:, i], scalar=RET_EPS, in1=den[:, i],
                                         op0=ALU.mult, op1=ALU.mult).then_inc(ready["den2"].sem, 1)
                dve.wait_ge(*ready["usq"](p, j))
                dve.tensor_reduce(ums[:, i], usq[:, i], X, ALU.add).then_inc(ready["ums"].sem, 1)
                dve.wait_ge(*ready["ums"](p, j))
                dve.scalar_tensor_tensor(out=uvar[:, i], in0=ums[:, i], scalar=1.0 / VD, in1=den2[:, i],
                                         op0=ALU.mult, op1=ALU.add).then_inc(ready["uvar"].sem, 1)

            def gate(p, par, b):
                for j in (2 * b, 2 * b + 1):
                    i = j % 2
                    dve.wait_ge(*ready["urs"](p, j))
                    dve.tensor_tensor(gated[:, i].rearrange("p (h v) -> p h v", h=HEADS), ug[:, i],
                                      urs[:, i].unsqueeze(2).broadcast_to([P, HEADS, VD]), ALU.mult)\
                       .then_inc(ready["gated"].sem, 1)

            def out_(p, par, b):
                tiles = slice(2 * b, 2 * b + 2)
                bank = c_filled(f"out{b}", p)
                if b == 0:
                    dve.reciprocal(crec[:], csum[:]).then_inc(ready["crec"].sem, 1)
                    dve.wait_ge(*ready["crec"](p))
                dve.tensor_tensor(z[:, tiles], bank[:, 0:2 * C].rearrange("p (j c) -> p j c", j=2),
                                  crec[:, tiles].unsqueeze(2).broadcast_to([P, 2, C]), ALU.mult)\
                   .then_inc(ready["z"].sem, 1)
                dve.wait_ge(*ready["zt"](p, b))
                dve.scalar_tensor_tensor(out=zt[:, tiles], in0=zt[:, tiles], scalar=1.0, in1=z[:, tiles],
                                         op0=ALU.add, op1=ALU.mult).then_inc(ready["zg"].sem, 1)

            def o(p, par, b):
                bank, filled, k = r_bank(f"o{b}")
                dve.wait_ge(*filled(p, k))
                dve.tensor_tensor(attn[:, 2 * b:2 * b + 2], bank[:, 0:2 * C].rearrange("p (j c) -> p j c", j=2),
                                  V["b_o"].unsqueeze(1).broadcast_to([P, 2, C]), ALU.add).then_inc(ready["attn"].sem, 1)
                if b == 0:
                    return
                dve.wait_ge(*ready["attn"](p, 1))
                dve.wait_ge(*ready["zg"](p, 1))
                dve.scalar_tensor_tensor(out=attn[:], in0=attn[:], scalar=0.5, in1=zt[:], op0=ALU.mult, op1=ALU.mult)\
                   .then_inc(ready["sg"].sem, 1)
                dve.wait_ge(*ready["sg"](p))
                dve.wait_ge(*stored(p))
                dve.tensor_tensor(x2[:], attn[:], x1[par][:], ALU.add).then_inc(ready["x2"].sem, 1)

            def head(p, u):
                if u >= UNITS:
                    return
                dve.wait_ge(*filled_s[u % 2](p, u // 2))
                if u >= MR:
                    g = u // 4 - MR // 4
                    _, filled, k = r_bank(f"g{g}")
                    dve.wait_ge(*filled(p, k))
                dve.tensor_tensor(ret[:, u % MR], bank_s[u % 2][:, 0:3 * P], causal, ALU.mult)\
                   .then_inc(ready["ret"].sem, 1)

            steps_of(dve, {"a_norm": a_norm, "a_xnT": a_xnT, "a_global": a_global, "a_srow": a_srow,
                           "a_score": a_score, "a_PT": a_PT, "a_local": a_local, "a_k": a_k, "a_v": a_v,
                           "a_gate": a_gate, "a_prod": a_prod, "a_xn2": a_xn2, "a_xn3": a_xn3, "qk": qk, "vg": vg,
                           "L": L, "LT": LT, "DT": DT, "h": h, "eo": eo, "row": row, "gate": gate, "out": out_,
                           "o": o}, head)

        @block.tensor
        def _(pe):
            pe.wait_ge(ready["slot_norm"].sem, 1)
            pe.wait_ge(loaded.sem, 64)
            for j in range(4):
                ins = pe.transpose(bank_r[1][:, j * P:(j + 1) * P], slot_sb[:, j], ident)
            ins.then_inc(filled_setup.sem, 1)
            pe.wait_ge(*ready["snT"](0))
            pe.wait_ge(loaded2.sem, 32)

            def a_claim(name, p):
                done, k, back = a_read(name)
                if not back:
                    pe.wait_ge(*done(p, k))
                elif not first(p):
                    pe.wait_ge(*done(p - 1, k))
                bank, filled, _ = a_bank(name)
                return bank, filled.sem

            def c_claim(name, p):
                done, k, back = c_read(name)
                if not back:
                    pe.wait_ge(*done(p, k))
                elif not first(p):
                    pe.wait_ge(*done(p - 1, k))
                bank, filled, _ = c_bank(name)
                return bank, filled.sem

            def r_claim(name, p):
                done, k, back = r_read(name)
                if not back:
                    pe.wait_ge(*done(p, k))
                elif not first(p):
                    pe.wait_ge(*done(p - 1, k))
                bank, filled, _ = r_bank(name)
                return bank, filled.sem

            def turn_tiles(bank, src, filled):
                for j in range(TILES):
                    ins = pe.transpose(bank[:, j * P:(j + 1) * P], src[:, j], ident)
                ins.then_inc(filled, 1)

            def a_xnT(p, par, k):
                pe.wait_ge(*ready["xn"](p))
                bank, filled = a_claim("xnT", p)
                turn_tiles(bank, xn, filled)

            def a_s(p, par, k):
                pe.wait_ge(*ready["xnT"](p))
                bank, filled = a_claim("s", p)
                pe.matmul(bank[:], W["spin"], xnT[:, :, 1:SEQ + 1], start=True, stop=True).then_inc(filled, 1)

            def a_global(p, par, k):
                pe.wait_ge(*ready["sT"](p))
                bank, filled = a_claim("global", p)
                pe.matmul(bank[:, 0:2], W["global"], s_sum[:], start=True, stop=True).then_inc(filled, 1)

            def a_e(p, par, k):
                bank, filled = a_claim("e", p)
                pe.matmul(bank[:], W["J"], sT[:], start=True, stop=True).then_inc(filled, 1)

            def a_srow(p, par, k):
                bank, filled = a_claim("srow", p)
                flat = sT[:].rearrange("p b n -> p (b n)")
                for j in range(TILES):
                    ins = pe.transpose(bank[:, j * P:(j + 1) * P], flat[:, j * P:(j + 1) * P], ident)
                ins.then_inc(filled, 1)

            def a_score(p, par, b):
                pe.wait_ge(*ready["eT"](p))
                bank, filled = a_claim(f"score{b}", p)
                for i in range(2):
                    j = 2 * b + i
                    ins = pe.matmul(bank[:, i * SEQ:(i + 1) * SEQ], eT[:, j * P:(j + 1) * P], sT[:, b],
                                    start=True, stop=True)
                ins.then_inc(filled, 1)

            def a_PT(p, par, m):
                pe.wait_ge(*ready["Pn"](p, 1))
                bank, filled = a_claim(f"PT{m}", p)
                for j in range(TILES):
                    ins = pe.transpose(bank[:, j * P:(j + 1) * P], prob[:, j, m * P:(m + 1) * P], ident)
                ins.then_inc(filled, 1)

            def a_local(p, par, k):
                pe.wait_ge(*ready["srow"](p))
                pe.wait_ge(*ready["PT"](p, 1))
                bank, filled = a_bank("local")[0], a_bank("local")[1].sem
                for b in range(2):
                    for m in range(2):
                        ins = pe.matmul(bank[:, b * SEQ:(b + 1) * SEQ], srow[:, 2 * b + m],
                                        probT[:, m, b * SEQ:(b + 1) * SEQ], start=(m == 0), stop=(m == 1))
                ins.then_inc(filled, 1)

            def a_r(p, par, k):
                pe.wait_ge(*ready["mix"](p))
                bank, filled = a_claim("r", p)
                pe.matmul(bank[:], W["r"], xrT, start=True, stop=True).then_inc(filled, 1)

            def a_k(p, par, k):
                bank, filled = a_claim("k", p)
                pe.matmul(bank[:], W["k"], xkT, start=True, stop=True).then_inc(filled, 1)

            def a_v(p, par, k):
                pe.wait_ge(*ready["ka"](p))
                bank, filled = a_claim("v", p)
                pe.matmul(bank[:], W["v"], kr, start=True, stop=True).then_inc(filled, 1)

            def a_prod(p, par, k):
                pe.wait_ge(*ready["prodT"](p))
                bank, filled = a_claim("prod", p)
                for j in range(TILES):
                    ins = pe.transpose(bank[:, j * P:(j + 1) * P], prodT[:, j * P:(j + 1) * P], ident)
                ins.then_inc(filled, 1)

            def a_xn2T(p, par, k):
                pe.wait_ge(*ready["xn2"](p))
                bank, filled = a_claim("xn2T", p)
                turn_tiles(bank, xn2, filled)

            def a_xn3T(p, par, k):
                pe.wait_ge(*ready["xn3"](p))
                bank, filled = a_claim("xn3T", p)
                turn_tiles(bank, xn3, filled)

            def qk(p, par, k):
                pe.wait_ge(*ready["xn2T"](p))
                bank, filled = c_claim(f"qk{k}", p)
                pe.matmul(bank[:], W[("q1", "k1")[k]], xn2T[:], start=True, stop=True).then_inc(filled, 1)

            def vg(p, par, j):
                bank, filled = c_claim(f"vg{j}", p)
                pe.matmul(bank[:], xn2T[:, j // 2, (j % 2) * P:(j % 2 + 1) * P], W["vg"], start=True, stop=True)\
                  .then_inc(filled, 1)

            def L(p, par, j):
                pe.wait_ge(*ready["xn3T"](p))
                bank, filled = c_claim(f"L{j}", p)
                pe.matmul(bank[:], xn3T[:, j * P:(j + 1) * P], snT[:], start=True, stop=True).then_inc(filled, 1)

            def LT(p, par, m):
                bank, filled = c_claim(f"LT{m}", p)
                pe.matmul(bank[:], snT[:, m * P:(m + 1) * P], xn3T[:], start=True, stop=True).then_inc(filled, 1)

            def CT(p, par, j):
                pe.wait_ge(*ready["Cexp"](p, j))
                bank, filled = c_claim(f"CT{j}", p)
                for m in range(4):
                    ins = pe.transpose(bank[:, m * P:(m + 1) * P], crow[:, j % 2, m * P:(m + 1) * P], ident)
                ins.then_inc(filled, 1)

            def DT(p, par, m):
                pe.wait_ge(*ready["DTn"](p, m))
                bank, filled = c_claim(f"DT{m}", p)
                for j in range(TILES):
                    ins = pe.transpose(bank[:, j * P:(j + 1) * P], dT[:, m, j // 2, (j % 2) * P:(j % 2 + 1) * P], ident)
                ins.then_inc(filled, 1)

            def slots(p, par, b):
                pe.wait_ge(*ready["D"](p, 3))
                bank, filled = c_claim(f"slots{b}", p)
                for i in range(2):
                    j = 2 * b + i
                    ins = pe.matmul(bank[:], xn3[:, j], d[:, j], start=(i == 0), stop=(i == 1))
                ins.then_inc(filled, 1)

            def h(p, par, e):
                pe.wait_ge(*ready["slotsT"](p, 1))
                bank, filled = c_claim(f"h{e}", p)
                for c in range(HC):
                    ins = pe.matmul(bank[:, c * P:(c + 1) * P], w1_sb[:, e, c * P:(c + 1) * P],
                                    slotsT[:, e].rearrange("p b s -> p (b s)"), start=True, stop=True)
                ins.then_inc(filled, 1)

            def eo(p, par, e):
                pe.wait_ge(*ready["hact"](p, e))
                bank, filled = c_claim(f"eo{e}", p)
                for c in range(HC):
                    ins = pe.matmul(bank[:, 0:P], w2_sb[:, e, c], hact[:, e % 2, c], start=(c == 0), stop=(c == HC - 1))
                ins.then_inc(filled, 1)

            def row(p, par, j):
                b, half = divmod(j, 2)
                pe.wait_ge(*ready["RT"](p, 4 * b + 3))
                bank, filled = r_claim(f"row{j}", p)
                for g in range(4):
                    ins = pe.transpose(bank[:, g * P:(g + 1) * P], RT[:, g, half * P:(half + 1) * P], ident)
                ins.then_inc(filled, 1)

            def gatedT_(p, par, b):
                pe.wait_ge(*ready["gated"](p, 2 * b + 1))
                bank, filled = r_claim(f"gatedT{b}", p)
                for i in range(2):
                    for v in range(2):
                        n = 2 * i + v
                        ins = pe.transpose(bank[:, n * P:(n + 1) * P], gated[:, i, v * P:(v + 1) * P], ident)
                ins.then_inc(filled, 1)

            def o(p, par, b):
                pe.wait_ge(*ready["gatedT"](p, b))
                bank, filled = r_claim(f"o{b}", p)
                for i in range(2):
                    for v in range(2):
                        ins = pe.matmul(bank[:, i * C:(i + 1) * C], (gatedT, gatedT2)[b][:, i, v],
                                        W["o"][:, v * C:(v + 1) * C], start=(v == 0), stop=(v == 1))
                ins.then_inc(filled, 1)

            def eorow_(p, par, b):
                pe.wait_ge(*ready["eoT"](p, E - 1))
                bank, filled = c_claim(f"eorow{b}", p)
                for m in range(4):
                    ins = pe.transpose(bank[:, m * P:(m + 1) * P],
                                       eoT[:, b, 2 * m:2 * m + 2].rearrange("p e s -> p (e s)"), ident)
                ins.then_inc(filled, 1)

            def out_(p, par, b):
                pe.wait_ge(*ready["eorow"](p, 1))
                bank, filled = c_claim(f"out{b}", p)
                for i in range(2):
                    j = 2 * b + i
                    for m in range(4):
                        ins = pe.matmul(bank[:, i * C:(i + 1) * C], cT[:, m, j * P:(j + 1) * P], eorow[:, b, m],
                                        start=(m == 0), stop=(m == 3))
                ins.then_inc(filled, 1)

            def head(p, u):
                if u < UNITS:
                    b = u // HEADS
                    pe.wait_ge(*ready["km"](p, u))
                    if u >= 2:
                        pe.wait_ge(*ready["ret"](p, u - 2))
                    elif not first(p):
                        pe.wait_ge(*ready["ret"](p - 1, u - 2 + UNITS))
                    bank = bank_s[u % 2]
                    pe.matmul(bank[:, 0:SEQ], km[:, u % KM, 0:P], qT[:, b], start=True, stop=True)
                    pe.matmul(bank[:, SEQ:SEQ + P], km[:, u % KM, P:SEQ], qT[:, b, P:SEQ], start=True, stop=True)\
                      .then_inc(filled_s[u % 2].sem, 1)
                if u >= 6 and (u - 6) % 4 == 0 and (u - 6) // 4 < UNITS // 4:
                    g = (u - 6) // 4
                    b = g // 4
                    pe.wait_ge(*ready["ret_abs"](p, 4 * g + 3))
                    pe.wait_ge(*ready["vg"](p, 2 * b + 1))
                    bank, filled = r_claim(f"g{g}", p)
                    for phase in range(4):
                        for i in range(4):
                            head = (4 * g + i) % HEADS
                            slot = (4 * g + i) % MR
                            src = (ret, ret_abs)[phase // 2]
                            sblock = phase % 2
                            left = vrow[:, 2 * b + sblock, head] if phase < 2 else K["count"]
                            cols = (0, SEQ) if sblock == 0 else (SEQ, 3 * P)
                            ins = pe.matmul(bank[i * HT:(i + 1) * HT, sblock * P:SEQ], left,
                                            src[:, slot, cols[0]:cols[1]], start=(phase == 0), stop=(phase == 3))
                    ins.then_inc(filled, 1)

            steps_of(pe, {"a_xnT": a_xnT, "a_s": a_s, "a_global": a_global, "a_e": a_e, "a_srow": a_srow,
                          "a_score": a_score, "a_PT": a_PT, "a_local": a_local, "a_r": a_r, "a_k": a_k, "a_v": a_v,
                          "a_prod": a_prod, "a_xn2T": a_xn2T, "a_xn3T": a_xn3T, "qk": qk, "vg": vg, "L": L, "LT": LT,
                          "CT": CT, "DT": DT, "slots": slots, "h": h, "eo": eo, "row": row, "gatedT": gatedT_,
                          "o": o, "eorow": eorow_, "out": out_}, head)


def _constants():
    k = np.zeros((P, K_N), np.float32)

    def put(name, a):
        k[:, slice(*K_COLS[name])] = a

    gamma = 1.0 - 2.0 ** (-5.0 - np.arange(HEADS))
    t = np.arange(SEQ)
    scale = np.sqrt((1.0 - gamma[:, None] ** (t + 1)) / (1.0 - gamma[:, None]))
    rows = np.arange(P) // KD
    put("ident", np.eye(P))
    put("qdecay", (gamma[:, None] ** t / scale)[rows])
    put("kdecay", (gamma[:, None] ** -t.astype(float))[rows])
    block = np.triu(np.ones((P, P)))
    put("causal", np.concatenate([block, np.ones((P, P)), block], 1))
    put("head", rows[:, None] == np.arange(HEADS)[None, :])
    put("count", (np.arange(HT) == VD)[None, :].repeat(P, 0))
    return k


def kernel(**inputs):
    import concourse.bacc as bacc
    from concourse.bass_utils import run_bass_kernel_spmd

    a = {n: np.ascontiguousarray(v) for n, v in inputs.items()}
    L0, L1 = "L0_attn_", "L1_attn_"
    qk = a[L1 + "W_qk"]
    w = np.empty((P, W_N), np.float32)
    for name, v in (("spin", a[L0 + "W_spin"].T), ("J", a[L0 + "W_J"].T), ("global", a[L0 + "W_global"].T),
                    ("r", a["L0_ffn_W_r"].T), ("k", a["L0_ffn_W_k"].T), ("v", a["L0_ffn_W_v"].T),
                    ("q1", qk[:, 0:C]), ("k1", qk[:, C:2 * C]),
                    ("vg", np.concatenate([a[L1 + "W_v"], a[L1 + "W_g"]], 1)),
                    ("o", a[L1 + "W_o"].reshape(2, P, C).transpose(1, 0, 2).reshape(P, 2 * C))):
        w[:, slice(*W_COLS[name])] = v
    v = np.empty((P, V_N), np.float32)
    for name, u in (("b_spin", a[L0 + "b_spin"][:, None]), ("mu_r", a["L0_ffn_mu_r"][:, None]),
                    ("mu_k", a["L0_ffn_mu_k"][:, None]), ("b_q", a[L1 + "b_qk"][0:C, None]),
                    ("b_k", a[L1 + "b_qk"][C:2 * C, None]), ("norm_gamma", a["L1_ffn_norm_gamma"][:, None]),
                    ("slot_gamma", a["L1_ffn_slot_norm_gamma"][:, None]),
                    ("beta", np.broadcast_to(a[L0 + "beta"], (P, 1))),
                    ("b1", a["L1_ffn_b1"].reshape(E * HC, P).T), ("b2", a["L1_ffn_b2"].T),
                    ("b_vg", np.broadcast_to(np.concatenate([a[L1 + "b_v"], a[L1 + "b_g"]]), (P, 2 * HEADS * VD))),
                    ("b_o", np.broadcast_to(a[L1 + "b_o"], (P, C)))):
        v[:, slice(*V_COLS[name])] = u
    x = a[L0 + "x"]
    arrays = {
        "x": x.reshape(-1, C), "weights": w, "vectors": v, "consts": _constants(),
        "w1": np.ascontiguousarray(a["L1_ffn_w1"].transpose(1, 0, 2)),
        "w2": np.ascontiguousarray(a["L1_ffn_w2"].reshape(E, HC, P, C).transpose(2, 0, 1, 3)),
        "slot_rows": np.ascontiguousarray(a["L1_ffn_slot_embeds"].reshape(4, P, C).transpose(1, 0, 2)),
    }
    nc = bacc.Bacc("TRN2", target_bir_lowering=False, num_devices=1)
    args = [nc.dram_tensor(n, u.shape, F32, kind="ExternalInput").ap() for n, u in arrays.items()]
    out = nc.dram_tensor("out", arrays["x"].shape, F32, kind="ExternalOutput").ap()
    build(nc, *args, out)
    r = run_bass_kernel_spmd(nc, [arrays], core_ids=[0])
    return r.results[0]["out"].reshape(x.shape)
```
